# Optimizing a Trainium2 kernel written in Bass

```python
import numpy as np
import jax
import jax.numpy as jnp

def _softmax(x, axis=-1):
    return jax.nn.softmax(x, axis=axis)

def _gelu(x):
    return jax.nn.gelu(x, approximate=True)

def _silu(x):
    return jax.nn.silu(x)

def _sigmoid(x):
    return jax.nn.sigmoid(x)

def _layernorm(x, axis=-1, eps=1e-05):
    m = jnp.mean(x, axis=axis, keepdims=True)
    v = jnp.var(x, axis=axis, keepdims=True)
    return (x - m) / jnp.sqrt(v + eps)

def _scatter_add(tgt, idx, src, axis=0):
    return tgt.at[idx].add(src)

def _segment_sum(src, seg, n):
    return jax.ops.segment_sum(src, seg, n)
kernel_name = 'mk_gnn_preln_d2_gnn_r8_48917a'

def setup_inputs(seed: int=0):
    np.random.seed(seed)
    _w = jnp.asarray

    def _rec_inputs():
        import jax
        import jax.numpy as jnp
        _gk = jax.random.key(seed)
        x = -0.0003713 + 1 * jax.random.normal(jax.random.fold_in(_gk, 1), (12500, 128), jnp.float32)
        src = jax.random.randint(jax.random.fold_in(_gk, 2), (200000,), 0, 12500, jnp.int32)
        dst = jnp.minimum((12500 * jax.random.uniform(jax.random.fold_in(_gk, 3), (200000,)) ** 2.0).astype(jnp.int32), 99999)
        _o = jnp.argsort(dst, stable=True)
        src = src[_o]
        dst = dst[_o]
        edge_attr_64 = -8.16379e-05 + 0.999858 * jax.random.normal(jax.random.fold_in(_gk, 12), (200000, 64), jnp.float32)
        edge_weight = jax.random.uniform(jax.random.fold_in(_gk, 14), (200000,), jnp.float32, 0.0, 0.999999)
        return (x, src, dst, edge_attr_64, edge_weight)
    x, src, dst, edge_attr_64, edge_weight = _rec_inputs()

    def _L0_gnn_setup():
        import jax, jax.numpy as jnp
        import numpy as np
        N_NODES = 12500
        N_EDGES = 200000
        IN_FEATS = 128
        OUT_FEATS = 128
        EDGE_HIDDEN = 64
        key = jax.random.key(seed)
        ks = jax.random.split(key, 7)
        h = jax.random.normal(ks[0], (N_NODES, IN_FEATS), dtype=jnp.float32)
        edge_feat = jax.random.normal(ks[1], (N_EDGES, EDGE_HIDDEN), dtype=jnp.float32)
        src = jax.random.randint(ks[2], (N_EDGES,), 0, N_NODES)
        dst = jax.random.randint(ks[3], (N_EDGES,), 0, N_NODES)
        stdv = 1.0 / np.sqrt(OUT_FEATS)
        stdv_e = 1.0 / np.sqrt(IN_FEATS)
        weight = jax.random.uniform(ks[4], (IN_FEATS, OUT_FEATS), minval=-stdv, maxval=stdv, dtype=jnp.float32)
        weight_edge = jax.random.uniform(ks[5], (EDGE_HIDDEN, IN_FEATS), minval=-stdv_e, maxval=stdv_e, dtype=jnp.float32)
        bias = jax.random.uniform(ks[6], (OUT_FEATS,), minval=-stdv, maxval=stdv, dtype=jnp.float32)
        return {'h': h, 'edge_feat': edge_feat, 'src': src, 'dst': dst, 'num_nodes': N_NODES, 'weight': weight, 'weight_edge': weight_edge, 'bias': bias}
    _L0_gnn_all = _L0_gnn_setup()
    _L0_gnn_in = {k: v for k, v in _L0_gnn_all.items() if k in ('weight', 'weight_edge', 'bias')}
    del _L0_gnn_all

    def _L1_gnn_setup():
        import jax, jax.numpy as jnp
        import numpy as np
        N = 12500
        E = 200000
        IN_CH = 128
        OUT_CH = 128

        def gcn_conv(x, edge_index, edge_weight, W, b):
            n = x.shape[0]
            loop_idx = jnp.arange(n, dtype=edge_index.dtype)
            row = jnp.concatenate([edge_index[0], loop_idx])
            col = jnp.concatenate([edge_index[1], loop_idx])
            w = jnp.concatenate([edge_weight, jnp.ones((n,), dtype=edge_weight.dtype)])
            deg = jax.ops.segment_sum(w, col, num_segments=n)
            dinv = jnp.where(deg > 0, jax.lax.rsqrt(deg), 0.0)
            norm = dinv[row] * w * dinv[col]
            xw = x @ W
            msgs = xw[row] * norm[:, None]
            out = jax.ops.segment_sum(msgs, col, num_segments=n)
            return out + b
        key = jax.random.key(seed)
        k1, k2, k3, k4, k5 = jax.random.split(key, 5)
        x = jax.random.normal(k1, (N, IN_CH), dtype=jnp.float32)
        edge_index = jax.random.randint(k2, (2, E), 0, N, dtype=jnp.int64)
        edge_weight = jax.random.uniform(k3, (E,), dtype=jnp.float32)
        W = jax.random.normal(k4, (IN_CH, OUT_CH), dtype=jnp.float32) / np.float32(np.sqrt(IN_CH))
        b = jnp.zeros((OUT_CH,), dtype=jnp.float32)
        return {'x': x, 'edge_index': edge_index, 'edge_weight': edge_weight, 'W': W, 'b': b}
    _L1_gnn_all = _L1_gnn_setup()
    _L1_gnn_in = {k: v for k, v in _L1_gnn_all.items() if k in ('W', 'b')}
    del _L1_gnn_all
    return {'x': x, 'src': src, 'dst': dst, 'edge_attr_64': edge_attr_64, 'edge_weight': edge_weight, 'L0_gnn_weight': _L0_gnn_in['weight'], 'L0_gnn_weight_edge': _L0_gnn_in['weight_edge'], 'L0_gnn_bias': _L0_gnn_in['bias'], 'L1_gnn_W': _L1_gnn_in['W'], 'L1_gnn_b': _L1_gnn_in['b']}

def reference(x, src, dst, edge_attr_64, edge_weight, L0_gnn_weight, L0_gnn_weight_edge, L0_gnn_bias, L1_gnn_W, L1_gnn_b):
    import jax
    import jax.numpy as jnp

    def _L0_gnn_ref(h, edge_feat, src, dst, num_nodes, weight, weight_edge, bias):
        import jax, jax.numpy as jnp
        import numpy as np
        N_NODES = 12500
        N_EDGES = 200000
        IN_FEATS = 128
        OUT_FEATS = 128
        EDGE_HIDDEN = 64
        eh = edge_feat @ weight_edge
        m = eh + h[src]
        agg = jax.ops.segment_sum(m, dst, num_segments=num_nodes)
        deg = jax.ops.segment_sum(jnp.ones((dst.shape[0],), dtype=h.dtype), dst, num_segments=num_nodes)
        norm = jnp.clip(deg, 1.0, None) ** (-0.5)
        agg = agg * norm[:, None]
        out = agg @ weight + bias
        return jax.nn.relu(out)

    def _L1_gnn_ref(x, edge_index, edge_weight, W, b):
        import jax, jax.numpy as jnp
        import numpy as np
        N = 12500
        E = 200000
        IN_CH = 128
        OUT_CH = 128

        def gcn_conv(x, edge_index, edge_weight, W, b):
            n = x.shape[0]
            loop_idx = jnp.arange(n, dtype=edge_index.dtype)
            row = jnp.concatenate([edge_index[0], loop_idx])
            col = jnp.concatenate([edge_index[1], loop_idx])
            w = jnp.concatenate([edge_weight, jnp.ones((n,), dtype=edge_weight.dtype)])
            deg = jax.ops.segment_sum(w, col, num_segments=n)
            dinv = jnp.where(deg > 0, jax.lax.rsqrt(deg), 0.0)
            norm = dinv[row] * w * dinv[col]
            xw = x @ W
            msgs = xw[row] * norm[:, None]
            out = jax.ops.segment_sum(msgs, col, num_segments=n)
            return out + b
        return jax.nn.relu(gcn_conv(x, edge_index, edge_weight, W, b))
    edge_index = jnp.stack([src, dst])
    h = jnp.maximum(_layernorm(x, axis=-1), 0.0)
    x = x + _L0_gnn_ref(h, edge_attr_64, src, dst, 12500, L0_gnn_weight, L0_gnn_weight_edge, L0_gnn_bias)
    h = jnp.maximum(_layernorm(x, axis=-1), 0.0)
    x = x + _L1_gnn_ref(h, edge_index, edge_weight, L1_gnn_W, L1_gnn_b)
    return x

_drawn_inputs = setup_inputs


def setup_inputs(seed=0):
    import zlib

    import numpy as np

    out = dict(_drawn_inputs(seed))
    spreads = {'L1_gnn_b': (0.0, 0.1)}
    factors = {}
    for name, (base, spread) in spreads.items():
        noise = np.random.default_rng([zlib.crc32(name.encode()), seed]).standard_normal(out[name].shape)
        drawn = base * np.exp(spread * noise) if base else spread * noise
        out[name] = jnp.asarray(drawn.astype(out[name].dtype))
    for name, factor in factors.items():
        out[name] = (out[name] * factor).astype(out[name].dtype)
    return out
```

```python
import concourse.bass as bass
from concourse import mybir
from contextlib import ExitStack


def gnn_two_layers(nc, x, src, dst, edge_attr, edge_w, w0, w0_edge, b0, w1, b1, out, h_tab, g_tab):
    f32 = mybir.dt.float32
    i32 = mybir.dt.int32
    ALU = mybir.AluOpType
    ACT = mybir.ActivationFunctionType
    AX = mybir.AxisListType

    P = 128
    N, D = x.shape
    E = src.shape[0]
    DE = edge_attr.shape[1]
    K = 4
    CH = K * P
    NC = E // CH
    TAIL = E - NC * CH
    TP = TAIL // K
    assert TP * K == TAIL and 0 < TP < P
    NCH = NC + 1
    U = 6
    IT = NC // U
    assert IT * U == NC
    EF = 3
    LEAD = 4
    TW = NCH + LEAD - 1
    DX = DE + 2
    NB = -(-N // P)
    NT = N - (NB - 1) * P
    NP = (NB + 1) * P
    G = 14
    NG = NB // G
    assert NG * G == NB
    H = G // 2
    RG = NC // P
    RR = NC - RG * P
    EPS = 1e-5

    ctx = ExitStack()
    with ctx:
        def sb(name, shape, dt=f32):
            return ctx.enter_context(nc.sbuf_tensor(name, shape, dt))

        def sem(name):
            return ctx.enter_context(nc.semaphore(name))

        agg = sb("agg", [P, 2, NP])
        xs = sb("xs", [P, NB, D])
        dst_tab = sb("dst_tab", [P, K, TW])
        src_tab = sb("src_tab", [P, K, TW])
        w_tab = sb("w_tab", [P, K, TW])
        ring = sb("ring", [P, U, K * D])
        ef = sb("ef", [P, EF, K * DE])
        es = sb("es", [P, EF, K, DX])
        S = sb("S", [P, 2, K, P])
        SX = sb("SX", [P, K, P])
        xrel = sb("xrel", [P, K])
        idx = sb("idx", [P, U, K], i32)
        meta = sb("meta", [1, NCH], i32)
        ident = sb("ident", [P, P])
        iota_i = sb("iota_i", [P, P], i32)
        w0_sb = sb("w0_sb", [P, D])
        w1_sb = sb("w1_sb", [P, D])
        we_sb = sb("we_sb", [DE, D])
        weT = sb("weT", [P, DE])
        wew = sb("wew", [P, D])
        b0_sb = sb("b0_sb", [P, D])
        b1_sb = sb("b1_sb", [P, D])
        stage = sb("stage", [P, 2, 2, P])
        tbuf = sb("tbuf", [P, 2, D])
        stats = sb("stats", [P, NB, 6])
        deg_rows = sb("deg_rows", [NB, 2, P])
        mn = sb("mn", [P, 5])
        mx = sb("mx", [P, 5])
        span = sb("span", [P, 5], i32)
        extra = sb("extra", [P, 5], i32)
        packed = sb("packed", [P, 5])
        v = sb("v", [P, 2, NB])
        r = sb("r", [P, 2, NB])
        q = sb("q", [P, 2, NB])
        norms = sb("norms", [P, 2, NB])
        scale = sb("scale", [P, NB])
        shift = sb("shift", [P, NB])

        RL = 5 * CH
        assert 4 * RL <= NP and RL <= U * K * D
        rows_di = agg[:, 1, 0:RL].bitcast(i32).rearrange("p (g e) -> p g e", g=5)
        rows_si = agg[:, 1, RL:2 * RL].bitcast(i32).rearrange("p (g e) -> p g e", g=5)
        rows_d = agg[:, 1, 2 * RL:3 * RL].rearrange("p (g e) -> p g e", g=5)
        rows_s = agg[:, 1, 3 * RL:4 * RL].rearrange("p (g e) -> p g e", g=5)
        rows_w = ring[:, :, :].rearrange("p u e -> p (u e)")[:, 0:RL].rearrange("p (g e) -> p g e", g=5)
        hbuf = agg[:, 0, 0:NB * P].rearrange("p (b d) -> p b d", d=D)
        gbuf = ring[:, :, :].rearrange("p u e -> p (u e)")[:, 0:G * D].rearrange("p (b d) -> p b d", d=D)

        bank = [ctx.enter_context(nc.psum_tensor(f"bank{i}", [P, 512], f32)) for i in range(8)]
        iota = bank[7][:, 0:P]
        win = [bank[0], bank[1]]
        winx = bank[2]
        tr = [bank[3], bank[4]]
        zb = [bank[3], bank[4]]
        gt = [bank[5], bank[6]]

        x_in = [sem(f"x_in{g}") for g in range(NG)]
        rows_zero = sem("rows_zero")
        x_zero = sem("x_zero")
        rows_in = sem("rows_in")
        consts_in = sem("consts_in")
        ident_ok = sem("ident_ok")
        iota_ok = sem("iota_ok")
        pads_ok = sem("pads_ok")
        iota_ps = sem("iota_ps")
        rows_f = sem("rows_f")
        meta_t = sem("meta_t")
        meta_ok = sem("meta_ok")
        tab_t = sem("tab_t")
        tab_ok = sem("tab_ok")
        dchain = sem("dchain")
        var_ok = sem("var_ok")
        sqrt_ok = sem("sqrt_ok")
        affine_ok = sem("affine_ok")
        h_ready = sem("h_ready")
        h_out = sem("h_out")
        agg_zero = sem("agg_zero")
        we_t = sem("we_t")
        we_tc = sem("we_tc")
        wew_t = sem("wew_t")
        wew_ok = sem("wew_ok")
        es_ones = sem("es_ones")
        ef_in = [sem(f"ef_in{i}") for i in range(EF)]
        es_ready = sem("es_ready")

        class Layer:

            def __init__(self, n):
                self.idx_ready = sem(f"idx_ready{n}")
                self.opened = sem(f"opened{n}")
                self.got = [sem(f"got{n}_{u}") for u in range(U)]
                self.s_ready = sem(f"s_ready{n}")
                self.win_ready = sem(f"win_ready{n}")
                self.added = sem(f"added{n}")
                self.xrel_ok = sem(f"xrel_ok{n}")
                self.sx_ready = sem(f"sx_ready{n}")
                self.winx_ready = sem(f"winx_ready{n}")
                self.addedx = sem(f"addedx{n}")

        L0, L1 = Layer(0), Layer(1)
        deg_moved = sem("deg_moved")
        deg_t = sem("deg_t")
        norms_ok = sem("norms_ok")
        staged = sem("staged")
        z_ready = sem("z_ready")
        t_ok = sem("t_ok")
        x1_ok = sem("x1_ok")
        st_ok = sem("st_ok")
        g_ready = sem("g_ready")
        g_out = [sem("g_out0"), sem("g_out1")]
        g_t = sem("g_t")
        g_seed = sem("g_seed")
        staged1 = sem("staged1")
        z1_ready = sem("z1_ready")
        t1_ok = sem("t1_ok")
        out_ok = sem("out_ok")
        out_done = sem("out_done")

        block = ctx.enter_context(nc.Block())

        def loop(eng, n, body, first=1):
            for i in range(first):
                body(i)
            with eng.Fori(first, n) as i:
                body(i)

        def ge(eng, s, val):
            if not (isinstance(val, int) and val <= 0):
                eng.wait_ge(s, val)

        xg = x[0:(NB - 1) * P, :].rearrange("(b p) d -> p b d", p=P)
        og = out[0:(NB - 1) * P, :].rearrange("(b p) d -> p b d", p=P)
        hg = h_tab.rearrange("(b p) d -> p b d", p=P)
        gg = g_tab.rearrange("(b p) d -> p b d", p=P)

        @block.sync
        def _(sp):
            sp.wait_ge(rows_zero, 3)
            for i, (rows, a) in enumerate(((rows_si, src), (rows_di, dst), (rows_w, edge_w))):
                sp.dma_start(rows[:, 0:RG, :], a[0:RG * P * CH].rearrange("(g c e) -> c g e", g=RG, c=P)
                             ).then_inc(rows_in, 16)
                sp.dma_start(rows[0:RR, RG, :], a[RG * P * CH:NC * CH].rearrange("(c e) -> c e", c=RR)
                             ).then_inc(rows_in, 16)
                sp.dma_start(rows[0:1, RG + 1, 0:TAIL], a[NC * CH:E].rearrange("(c e) -> c e", c=1)
                             ).then_inc(rows_in, 16)
                sp.dma_start(rows[0:1, RG + 1, TAIL:CH], a[E - CH + TAIL:E].rearrange("(c e) -> c e", c=1)
                             ).then_inc(rows_in, 16)
            for g in range(NG):
                lo, hi = g * G, min((g + 1) * G, NB - 1)
                sp.dma_start(xs[:, lo:hi, :], xg[:, lo:hi, :]).then_inc(x_in[g], 16)
            sp.wait_ge(x_zero, 1)
            sp.dma_start(xs[0:NT, NB - 1, :], x[(NB - 1) * P:N, :]).then_inc(x_in[NG - 1], 16)
            sp.dma_start(w0_sb[:, :], w0).then_inc(consts_in, 16)
            sp.dma_start(w1_sb[:, :], w1).then_inc(consts_in, 16)
            sp.dma_start(we_sb[:, :], w0_edge).then_inc(consts_in, 16)
            sp.dma_start(b0_sb[:, :], b0.partition_broadcast(P)).then_inc(consts_in, 16)
            sp.dma_start(b1_sb[:, :], b1.partition_broadcast(P)).then_inc(consts_in, 16)
            for g in range(NG):
                sp.wait_ge(h_ready, (g + 1) * G)
                sp.dma_start(hg[:, g * G:(g + 1) * G, :], hbuf[:, g * G:(g + 1) * G, :]).then_inc(h_out, 16)

            def ef_load(c, u):
                ge(sp, es_ready, 2 * (c - EF + 1))
                sp.dma_start(ef[:, u % EF, :], edge_attr[bass.ds(c * CH, CH), :]
                             .rearrange("(p k) d -> p (k d)", k=K)).then_inc(ef_in[u % EF], 16)

            loop(sp, IT, lambda i: [ef_load(i * U + u, u) for u in range(U)])
            sp.wait_ge(es_ready, 2 * (NC - EF + 1))
            sp.dma_start(ef[0:TP, 0, :], edge_attr[NC * CH:E, :].rearrange("(p k) d -> p (k d)", k=K)
                         ).then_inc(ef_in[0], 16)
            sp.wait_ge(L0.added, 2 * NCH)
            for j in range(2):
                sp.dma_start(deg_rows[:, j, :], agg[DE + j:DE + j + 1, 1, 0:NB * P]
                             .rearrange("o (b n) -> o b n", b=NB)).then_inc(deg_moved, 16)

            def g_store(i):
                for j in range(2):
                    sp.wait_ge(g_ready, i * G + (j + 1) * H)
                    sp.dma_start(gg[:, bass.ds(i * G + j * H, H), :], gbuf[:, j * H:(j + 1) * H, :]
                                 ).then_inc(g_out[j], 16)

            loop(sp, NG, g_store)
            for g in range(NG):
                lo, hi = g * G, min((g + 1) * G, NB - 1)
                sp.wait_ge(out_ok, (g + 1) * G)
                sp.dma_start(og[:, lo:hi, :], xs[:, lo:hi, :]).then_inc(out_done, 16)
            sp.dma_start(out[(NB - 1) * P:N, :], xs[0:NT, NB - 1, :]).then_inc(out_done, 16)
            sp.wait_ge(out_done, (NG + 1) * 16)

        @block.gpsimd
        def _(pool):
            pool.memset(xs[:, NB - 1, :], 0.0).then_inc(x_zero, 1)
            for rows in (rows_si, rows_di, rows_w):
                pool.memset(rows[:, RG:RG + 2, :], 0).then_inc(rows_zero, 1)
            pool.memset(ident[:, :], 0.0).then_inc(ident_ok, 1)
            pool.wait_ge(ident_ok, 1)
            pool.affine_select(out=ident[:, :], in_=ident[:, :], compare_op=ALU.not_equal, fill=1.0,
                               base=0, pattern=[[-1, P]], channel_multiplier=1).then_inc(ident_ok, 1)
            pool.iota(iota_i[:, :], pattern=[[1, P]], base=0, channel_multiplier=0).then_inc(iota_ok, 1)
            pool.memset(es[:, :, :, :], 1.0).then_inc(es_ones, 1)
            for tab in (dst_tab, src_tab, w_tab):
                pool.memset(tab[:, :, NCH:TW], 0.0).then_inc(pads_ok, 1)
            pool.memset(wew[:, :], 0.0).then_inc(pads_ok, 1)

            def gathers(L, table, c, u, rows, added):
                pool.wait_ge(L.idx_ready, c + 1)
                ge(pool, L.added, added * (c - U + 1))
                pool.sem_inc(L.opened, 1)
                for k in range(K):
                    pool.indirect_dma_start(
                        ring[0:rows, u, k * D:(k + 1) * D], None, table[:, :],
                        bass.IndirectOffsetOnAxis(ap=idx[0:rows, u, k:k + 1], axis=0),
                    ).then_inc(L.got[u], 16)

            for L, table, done, added in ((L0, h_tab, [(h_out, 16 * NG)], 2),
                                          (L1, g_tab, [(g_out[0], 16 * NG), (g_out[1], 16 * NG)], 1)):
                for s, n in done:
                    pool.wait_ge(s, n)
                if L is L1:
                    pool.wait_ge(g_t, 2 * NG)
                loop(pool, IT, lambda i: [gathers(L, table, i * U + u, u, P, added) for u in range(U)])
                gathers(L, table, NC, 0, TP, added)

        @block.scalar
        def _(act):
            act.wait_ge(pads_ok, 4)
            for n in range(3 * K):
                act.wait_ge(tab_t, n + 1)
                tab = (src_tab, dst_tab, w_tab)[n // K]
                act.activation(tab[:, n % K, 0:NCH], tr[n % 2][:, 0:NCH], ACT.Copy).then_inc(tab_ok, 1)
            act.wait_ge(we_t, 1)
            act.activation(weT[:, :], gt[0][:, 0:DE], ACT.Copy).then_inc(we_tc, 1)
            act.wait_ge(wew_t, 1)
            act.activation(wew[0:DE, :], gt[1][0:DE, 0:D], ACT.Copy).then_inc(wew_ok, 1)
            act.wait_ge(var_ok, 1)
            act.activation(q[:, 0, :], v[:, 0, :], ACT.Sqrt).then_inc(sqrt_ok, 1)
            act.wait_ge(affine_ok, 1)
            for g in range(NG):
                with act.Fori(g * G, (g + 1) * G) as b:
                    act.activation(hbuf[:, bass.ds(b, 1), :], xs[:, bass.ds(b, 1), :], ACT.Relu,
                                   bias=shift[:, bass.ds(b, 1)], scale=scale[:, bass.ds(b, 1)]
                                   ).then_inc(h_ready, 1)

            def stage_idx(L, c, u):
                s = u % U
                act.activation(idx[:, s, :], src_tab[:, :, bass.ds(c, 1)].rearrange("p k o -> p (k o)"),
                               ACT.Copy).then_inc(L.idx_ready, 1)

            def step(L, i, u):
                c = i * U + u
                if L is L0:
                    ge(act, L0.added, 2 * (c - EF + 1))
                    act.wait_ge(ef_in[u % EF], 16 * (i * (U // EF) + u // EF + 1))
                    act.activation(es[:, u % EF, :, 0:DE], ef[:, u % EF, :].rearrange("p (k d) -> p k d", k=K),
                                   ACT.Copy).then_inc(es_ready, 1)
                    act.activation(es[:, u % EF, :, DE + 1:DX], w_tab[:, :, bass.ds(c, 1)], ACT.Copy
                                   ).then_inc(es_ready, 1)
                before = u + LEAD - U
                if before >= 0:
                    act.wait_ge(L.got[before], 16 * K * (i + 1))
                elif not (isinstance(i, int) and i == 0):
                    act.wait_ge(L.got[before + U], 16 * K * i)
                stage_idx(L, c + LEAD, u + LEAD)

            def tail_cols():
                act.wait_ge(L0.added, 2 * (NC - EF + 1))
                act.wait_ge(ef_in[0], 16 * (IT * (U // EF) + 1))
                act.activation(es[0:TP, 0, :, 0:DE], ef[0:TP, 0, :].rearrange("p (k d) -> p k d", k=K),
                               ACT.Copy).then_inc(es_ready, 1)
                act.activation(es[0:TP, 0, :, DE + 1:DX], w_tab[0:TP, :, NC:NC + 1], ACT.Copy
                               ).then_inc(es_ready, 1)

            act.wait_ge(tab_ok, 3 * K)
            act.wait_ge(es_ones, 1)
            for c in range(LEAD):
                stage_idx(L0, c, c)
            loop(act, IT, lambda i: [step(L0, i, u) for u in range(U)])
            tail_cols()

            act.wait_ge(var_ok, 2)
            act.activation(q[:, :, :], v[:, :, :], ACT.Sqrt).then_inc(sqrt_ok, 1)

            def stage_block(i):
                for j in range(2):
                    b = i * 2 + j
                    ge(act, z_ready, b - 1)
                    act.activation(stage[:, j, :, :], agg[:, :, bass.ds(b * P, P)], ACT.Copy
                                   ).then_inc(staged, 1)

            loop(act, NB // 2, stage_block)
            act.wait_ge(var_ok, 3)
            act.activation(q[:, 0, :], v[:, 0, :], ACT.Sqrt).then_inc(sqrt_ok, 1)
            act.wait_ge(affine_ok, 2)
            act.wait_ge(L0.added, 2 * NCH)

            def g_rows(i):
                for j in range(G):
                    if j % H == 0:
                        ge(act, g_out[j // H], 16 * i)
                        ge(act, g_t, 2 * (i - 1) + j // H + 1)
                    b = i * G + j
                    act.activation(gbuf[:, j:j + 1, :], xs[:, bass.ds(b, 1), :], ACT.Relu,
                                   bias=shift[:, bass.ds(b, 1)], scale=scale[:, bass.ds(b, 1)]
                                   ).then_inc(g_ready, 1)

            loop(act, NG, g_rows)

            for c in range(LEAD):
                stage_idx(L1, c, c)
            loop(act, IT, lambda i: [step(L1, i, u) for u in range(U)])

            def stage_block1(i):
                for j in range(2):
                    b = i * 2 + j
                    ge(act, z1_ready, b - 1)
                    act.activation(stage[:, j, 0, :], agg[:, 0, bass.ds(b * P, P)], ACT.Copy
                                   ).then_inc(staged1, 1)

            act.wait_ge(L1.added, NCH)
            loop(act, NB // 2, stage_block1)

        @block.vector
        def _(dve):
            links = [0]

            def link(ins):
                links[0] += 1
                ins.then_inc(dchain, 1)
                dve.wait_ge(dchain, links[0])

            def group_stats(g):
                with dve.Fori(g * G, (g + 1) * G) as b:
                    dve.bn_stats(stats[:, bass.ds(b, 1), :].rearrange("p o s -> p (o s)"),
                                 xs[:, bass.ds(b, 1), :].rearrange("p o d -> p (o d)")
                                 ).then_inc(st_ok, 1)

            def variances(n):
                dve.wait_ge(st_ok, n * NB)
                even, odd = stats[:, :, 1], stats[:, :, 4]
                nc.vector.tensor_tensor(q[:, 1, :], even, odd, ALU.add)
                nc.vector.tensor_tensor(r[:, 1, :], even, odd, ALU.subtract)
                link(nc.vector.tensor_tensor(v[:, 1, :], stats[:, :, 2], stats[:, :, 5], ALU.add))
                nc.vector.tensor_scalar(v[:, 0, :], v[:, 1, :], 1.0 / D, EPS, ALU.mult, ALU.add)
                link(nc.vector.tensor_tensor(r[:, 0, :], r[:, 1, :], r[:, 1, :], ALU.mult))
                nc.vector.scalar_tensor_tensor(out=v[:, 0, :], in0=r[:, 0, :], scalar=0.25, in1=v[:, 0, :],
                                               op0=ALU.mult, op1=ALU.add).then_inc(var_ok, 1)

            def rsqrt(n, vv, rr, qq):
                dve.wait_ge(sqrt_ok, n)
                link(nc.vector.reciprocal(rr, qq))
                link(nc.vector.tensor_tensor(qq, rr, rr, ALU.mult))
                link(nc.vector.tensor_tensor(qq, qq, vv, ALU.mult))
                link(nc.vector.tensor_scalar(qq, qq, -0.5, 1.5, ALU.mult, ALU.add))
                link(nc.vector.tensor_tensor(rr, rr, qq, ALU.mult))

            dve.wait_ge(rows_in, 12 * 16)
            nc.vector.tensor_copy(rows_s, rows_si).then_inc(rows_f, 1)
            link(nc.vector.tensor_copy(rows_d, rows_di))
            nc.vector.tensor_reduce(mn[:, :], rows_d, AX.X, ALU.min)
            link(nc.vector.tensor_reduce(mx[:, :], rows_d, AX.X, ALU.max))
            link(nc.vector.tensor_tensor(span[:, :], mx[:, :], mn[:, :], ALU.subtract))
            link(nc.vector.tensor_scalar(extra[:, :], span[:, :], 7, None, ALU.arith_shift_right))
            nc.vector.scalar_tensor_tensor(out=packed[:, :], in0=mn[:, :], scalar=float(P), in1=extra[:, :],
                                           op0=ALU.mult, op1=ALU.add).then_inc(rows_f, 1)
            for g in range(5):
                last = nc.vector.tensor_scalar(rows_d[:, g, :], rows_d[:, g, :], mn[:, g:g + 1], None,
                                               ALU.subtract)
            last.then_inc(rows_f, 1)
            dve.wait_ge(iota_ok, 1)
            nc.vector.tensor_copy(iota, iota_i[:, :]).then_inc(iota_ps, 1)
            for g in range(NG):
                dve.wait_ge(x_in[g], 16 if g < NG - 1 else 32)
                group_stats(g)
            variances(1)
            dve.wait_ge(meta_t, 1)
            nc.vector.tensor_copy(meta[:, :], gt[0][0:1, 0:NCH]).then_inc(meta_ok, 1)
            rsqrt(1, v[:, 0, :], r[:, 0, :], q[:, 0, :])
            nc.vector.tensor_copy(scale[:, :], r[:, 0, :])
            nc.vector.scalar_tensor_tensor(out=shift[:, :], in0=q[:, 1, :], scalar=-0.5, in1=r[:, 0, :],
                                           op0=ALU.mult, op1=ALU.mult).then_inc(affine_ok, 1)
            dve.wait_ge(tab_t, 3 * K)
            nc.vector.memset(agg[:, 1, :], 0.0).then_inc(agg_zero, 1)
            dve.wait_ge(h_out, 16 * NG)
            nc.vector.memset(agg[:, 0, :], 0.0).then_inc(agg_zero, 1)

            extras = dve.alloc_register("extras_seen")
            writes = dve.alloc_register("xrel_writes")
            start = dve.alloc_register("window_start")
            startx = dve.alloc_register("extra_window_start")

            def one_hot(L, dest, rel):
                for k in range(K):
                    d, w = rel(k)
                    if L is L0:
                        last = nc.vector.tensor_scalar(dest[:, k, :], iota, d, None, ALU.is_equal)
                    else:
                        last = nc.vector.tensor_scalar(dest[:, k, :], iota, d, w, ALU.is_equal, ALU.mult)
                return last

            def add_window(L, at, ps, s):
                ops = [(D, 0)] if L is L1 else [(D, 0), (DX, 1)]
                for rows, plane in ops:
                    w = agg[0:rows, plane, bass.ds(at, P)]
                    nc.vector.tensor_tensor(w, w, ps[0:rows, plane * P:(plane + 1) * P], ALU.add).then_inc(s, 1)

            def build(L, c, u):
                ge(dve, L.win_ready, c - 1)
                col = bass.ds(c, 1)
                one_hot(L, S[:, u % 2], lambda k: (dst_tab[:, k, col], w_tab[:, k, col])).then_inc(L.s_ready, 1)

            def finish(L, c, u, packed_c):
                adds = 2 if L is L0 else 1
                n = packed_c & (P - 1)
                dve.reg_mov(start, packed_c >> 7)
                at = dve.snap(start, min_val=0, max_val=N - 1)
                ge(dve, L.added, adds * c)
                col = bass.ds(c, 1)
                with dve.If(n > 0):
                    nc.vector.tensor_copy(xrel[:, :], dst_tab[:, :, col].rearrange("p k o -> p (k o)")
                                          ).then_inc(L.xrel_ok, 1)
                    dve.reg_add(writes, writes, 1)
                    dve.reg_mov(startx, start)
                    with dve.Fori(0, n):
                        dve.wait_ge(L.xrel_ok, dve.snap(writes, min_val=1))
                        nc.vector.tensor_scalar(xrel[:, :], xrel[:, :], float(-P), None, ALU.add
                                                ).then_inc(L.xrel_ok, 1)
                        dve.reg_add(writes, writes, 1)
                        dve.reg_add(extras, extras, 1)
                        dve.reg_add(startx, startx, P)
                        dve.wait_ge(L.xrel_ok, dve.snap(writes, min_val=1))
                        one_hot(L, SX, lambda k: (xrel[:, k:k + 1], w_tab[:, k, col])).then_inc(L.sx_ready, 1)
                        dve.wait_ge(L.winx_ready, dve.snap(extras, min_val=1))
                        add_window(L, dve.snap(startx, min_val=0, max_val=N - 1), winx, L.addedx)
                with dve.Else():
                    pass
                dve.wait_ge(L.win_ready, c + 1)
                add_window(L, at, win[u % 2], L.added)

            def edge_loop(L):
                dve.reg_mov(extras, 0)
                dve.reg_mov(writes, 0)

                def body(i):
                    vals = [dve.value_load(meta[0:1, bass.ds(i * U + u, 1)], min_val=0, max_val=N * P)
                            for u in range(U)]
                    build(L, i * U, 0)
                    for u in range(U):
                        if u + 1 < U:
                            build(L, i * U + u + 1, u + 1)
                        finish(L, i * U + u, u, vals[u])

                loop(dve, IT, body)
                val = dve.value_load(meta[0:1, NC:NC + 1], min_val=0, max_val=N * P)
                build(L, NC, 0)
                finish(L, NC, 0, val)

            dve.wait_ge(meta_ok, 1)
            dve.wait_ge(tab_ok, 3 * K)
            dve.wait_ge(iota_ps, 1)
            dve.wait_ge(agg_zero, 2)
            edge_loop(L0)

            dve.wait_ge(deg_t, 1)
            link(nc.vector.tensor_scalar(r[:, 1, :], gt[0][:, NB:2 * NB], 1.0, None, ALU.add))
            nc.vector.tensor_scalar(v[:, 0, :], gt[0][:, 0:NB], 1.0, None, ALU.max)
            nc.vector.tensor_scalar(v[:, 1, :], r[:, 1, :], 1e-30, None, ALU.max).then_inc(var_ok, 1)
            link(nc.vector.tensor_scalar(scale[:, :], r[:, 1, :], 0.0, None, ALU.is_gt))
            rsqrt(2, v[:, :, :], r[:, :, :], q[:, :, :])
            nc.vector.tensor_copy(norms[:, 0, :], r[:, 0, :])
            link(nc.vector.tensor_tensor(norms[:, 1, :], r[:, 1, :], scale[:, :], ALU.mult))

            def z_affine(zs, ts, used, which, bias, b, j):
                ge(dve, used, b - 1)
                dve.wait_ge(zs, b + 1)
                nc.vector.scalar_tensor_tensor(out=tbuf[:, j, :], in0=zb[j][:, 0:D],
                                               scalar=norms[:, which, bass.ds(b, 1)], in1=bias[:, :],
                                               op0=ALU.mult, op1=ALU.add).then_inc(ts, 1)

            def relu_add(ts, s, b, j):
                dve.wait_ge(ts, b + 1)
                xb = xs[:, bass.ds(b, 1), :].rearrange("p o d -> p (o d)")
                nc.vector.scalar_tensor_tensor(out=xb, in0=tbuf[:, j, :], scalar=0.0, in1=xb,
                                               op0=ALU.max, op1=ALU.add).then_inc(s, 1)

            def block_stats(b):
                dve.wait_ge(x1_ok, b + 1)
                nc.vector.bn_stats(stats[:, bass.ds(b, 1), :].rearrange("p o s -> p (o s)"),
                                   xs[:, bass.ds(b, 1), :].rearrange("p o d -> p (o d)")).then_inc(st_ok, 1)

            dve.wait_ge(consts_in, 5 * 16)

            def mid(i):
                for j in range(2):
                    b = i * 2 + j
                    z_affine(z_ready, t_ok, x1_ok, 0, b0_sb, b, j)
                    if not (isinstance(b, int) and b == 0):
                        relu_add(t_ok, x1_ok, b - 1, 1 - j)
                        if not (isinstance(b, int) and b == 1):
                            block_stats(b - 2)

            loop(dve, NB // 2, mid)
            relu_add(t_ok, x1_ok, NB - 1, 1)
            block_stats(NB - 2)
            block_stats(NB - 1)
            variances(2)
            rsqrt(3, v[:, 0, :], r[:, 0, :], q[:, 0, :])
            link(nc.vector.tensor_tensor(scale[:, :], r[:, 0, :], norms[:, 1, :], ALU.mult))
            nc.vector.scalar_tensor_tensor(out=shift[:, :], in0=q[:, 1, :], scalar=-0.5, in1=scale[:, :],
                                           op0=ALU.mult, op1=ALU.mult).then_inc(affine_ok, 1)

            def seed(i):
                for j in range(2):
                    dve.wait_ge(g_t, 2 * i + j + 1)
                    b = i * G + j * H
                    nc.vector.tensor_copy(agg[:, 0, bass.ds(b * P, 4 * P)], gt[0][:, :]).then_inc(g_seed, 1)
                    nc.vector.tensor_copy(agg[:, 0, bass.ds((b + 4) * P, 3 * P)], gt[1][:, 0:3 * P]
                                          ).then_inc(g_seed, 1)

            loop(dve, NG, seed)
            dve.wait_ge(g_seed, 4 * NG)
            edge_loop(L1)

            def fin(i):
                for j in range(2):
                    b = i * 2 + j
                    z_affine(z1_ready, t1_ok, out_ok, 1, b1_sb, b, j)
                    if not (isinstance(b, int) and b == 0):
                        relu_add(t1_ok, out_ok, b - 1, 1 - j)

            loop(dve, NB // 2, fin)
            relu_add(t1_ok, out_ok, NB - 1, 1)

        @block.tensor
        def _(pe):
            mm = nc.tensor.matmul
            pe.wait_ge(ident_ok, 2)
            pe.wait_ge(rows_f, 3)
            groups = [(g, P) for g in range(RG)] + [(RG, RR), (RG + 1, 1)]
            place = [0, P, 2 * P, RG * P, NC]
            for g, n in groups:
                last = nc.tensor.transpose(gt[0][0:1, place[g]:place[g] + n], packed[0:n, g:g + 1],
                                           ident[0:n, 0:n])
            last.then_inc(meta_t, 1)
            for n in range(3 * K):
                rows, k = (rows_s, rows_d, rows_w)[n // K], n % K
                ge(pe, tab_ok, n - 1)
                for g, m in groups:
                    last = nc.tensor.transpose(tr[n % 2][:, place[g]:place[g] + m],
                                               rows[0:m, g, :].rearrange("c (p k) -> c k p", k=K)[:, k, :],
                                               ident[0:m, 0:m])
                last.then_inc(tab_t, 1)
            pe.wait_ge(consts_in, 5 * 16)
            pe.wait_ge(meta_ok, 1)
            nc.tensor.transpose(gt[0][:, 0:DE], we_sb[:, :], ident[0:DE, 0:DE]).then_inc(we_t, 1)
            pe.wait_ge(we_tc, 1)
            mm(gt[1][0:DE, 0:D], weT[:, :], w0_sb[:, :], start=True, stop=True).then_inc(wew_t, 1)

            extras = pe.alloc_register("extras_done")

            def sums(L, ps, slot, ti, tiles, rows, s):
                for k in range(K):
                    last = mm(ps[:, 0:P], ring[0:rows, slot, k * D:(k + 1) * D], tiles[0:rows, k, :],
                              start=(k == 0), stop=(k == K - 1))
                if L is L0:
                    for k in range(K):
                        last = mm(ps[0:DX, P:2 * P], es[0:rows, ti, k, :], tiles[0:rows, k, :],
                                  start=(k == 0), stop=(k == K - 1))
                last.then_inc(s, 1)

            def chunk(L, c, u, rows, fills, val):
                n = val & (P - 1)
                pe.wait_ge(L.got[u], 16 * K * fills)
                if L is L0:
                    pe.wait_ge(es_ready, 2 * (c + 1))
                pe.wait_ge(L.s_ready, c + 1)
                ge(pe, L.added, (2 if L is L0 else 1) * (c - 1))
                sums(L, win[u % 2], u, u % EF, S[:, u % 2], rows, L.win_ready)
                with pe.If(n > 0):
                    with pe.Fori(0, n):
                        pe.reg_add(extras, extras, 1)
                        pe.wait_ge(L.sx_ready, pe.snap(extras, min_val=1))
                        sums(L, winx, u, u % EF, SX, rows, L.winx_ready)
                with pe.Else():
                    pass

            def edge_loop(L):
                pe.reg_mov(extras, 0)

                def body(i):
                    vals = [pe.value_load(meta[0:1, bass.ds(i * U + u, 1)], min_val=0, max_val=N * P)
                            for u in range(U)]
                    for u in range(U):
                        chunk(L, i * U + u, u, P, i + 1, vals[u])

                loop(pe, IT, body)
                val = pe.value_load(meta[0:1, NC:NC + 1], min_val=0, max_val=N * P)
                chunk(L, NC, 0, TP, IT + 1, val)

            edge_loop(L0)

            pe.wait_ge(deg_moved, 32)
            for j in range(2):
                last = nc.tensor.transpose(gt[0][:, j * NB:(j + 1) * NB], deg_rows[:, j, :], ident[0:NB, 0:NB])
            last.then_inc(deg_t, 1)
            pe.wait_ge(wew_ok, 1)

            def mid(i):
                for j in range(2):
                    b = i * 2 + j
                    pe.wait_ge(staged, b + 1)
                    ge(pe, t_ok, b - 1)
                    mm(zb[j][:, 0:D], stage[:, j, 0, :], w0_sb[:, :], start=True, stop=False)
                    mm(zb[j][:, 0:D], stage[:, j, 1, :], wew[:, :], start=False, stop=True).then_inc(z_ready, 1)

            loop(pe, NB // 2, mid)

            def g_transpose(i):
                for j in range(2):
                    pe.wait_ge(g_ready, i * G + (j + 1) * H)
                    ge(pe, g_seed, 2 * (2 * i + j))
                    for m in range(H):
                        last = nc.tensor.transpose(gt[m // 4][:, (m % 4) * P:(m % 4 + 1) * P],
                                                   gbuf[:, j * H + m, :], ident[:, :])
                    last.then_inc(g_t, 1)

            loop(pe, NG, g_transpose)
            edge_loop(L1)

            def last_product(i):
                for j in range(2):
                    b = i * 2 + j
                    pe.wait_ge(staged1, b + 1)
                    ge(pe, t1_ok, b - 1)
                    mm(zb[j][:, 0:D], stage[:, j, 0, :], w1_sb[:, :], start=True, stop=True).then_inc(z1_ready, 1)

            loop(pe, NB // 2, last_product)


_INS = ["x", "src", "dst", "edge_attr_64", "edge_weight", "L0_gnn_weight", "L0_gnn_weight_edge", "L0_gnn_bias",
        "L1_gnn_W", "L1_gnn_b"]


def kernel(**inputs):
    import numpy as _np
    import concourse.bacc as _bacc
    from concourse import mybir as _mybir
    from concourse.bass_utils import run_bass_kernel_spmd as _run

    nc = _bacc.Bacc("TRN2", target_bir_lowering=False, num_devices=1)
    arrays, args = {}, []
    for name in _INS:
        a = _np.ascontiguousarray(inputs[name])
        arrays[f"in_{name}"] = a
        args.append(nc.dram_tensor(f"in_{name}", a.shape, _mybir.dt.from_np(a.dtype), kind="ExternalInput").ap())
    n, d = inputs["x"].shape
    args.append(nc.dram_tensor("out_x", (n, d), _mybir.dt.float32, kind="ExternalOutput").ap())
    padded = -(-n // 128) * 128
    for name in ("h_table", "g_table"):
        args.append(nc.dram_tensor(name, (padded, d), _mybir.dt.float32).ap())
    gnn_two_layers(nc, *args)
    r = _run(nc, [arrays], core_ids=[0])
    return r.results[0]["out_x"]
```

```python
import concourse.bass as bass
from concourse import mybir
from contextlib import ExitStack


def gnn_two_layers(nc, x, src, dst, edge_attr, edge_w, w0, w0_edge, b0, w1, b1, out, h_tab, g_tab):
    f32 = mybir.dt.float32
    i32 = mybir.dt.int32
    ALU = mybir.AluOpType
    ACT = mybir.ActivationFunctionType
    AX = mybir.AxisListType

    P = 128
    N, D = x.shape
    E = src.shape[0]
    DE = edge_attr.shape[1]
    K = 4
    CH = K * P
    NC = E // CH
    TAIL = E - NC * CH
    TP = TAIL // K
    assert TP * K == TAIL and 0 < TP < P
    NCH = NC + 1
    U = 10
    IT = NC // U
    assert IT * U == NC
    EF = 2
    ES = 2
    IL = 6
    HU = U // 2
    DX = DE + 2
    NB = -(-N // P)
    NT = N - (NB - 1) * P
    NP = (NB + 1) * P
    G = 7
    NG = NB // G
    assert NG * G == NB
    G4 = 4
    CUTS = [0, G, 3 * G, 7 * G, 11 * G, NB]
    NBT = len(CUTS) - 1
    PB = 5
    LB = 2
    HT = HU * K
    NM = IT + 1
    PAD = 64
    assert all((t * 147) >> 10 == t // G for t in range(NB + 1))
    RG = NC // P
    RR = NC - RG * P
    EPS = 1e-5

    ctx = ExitStack()
    with ctx:
        def sb(name, shape, dt=f32):
            return ctx.enter_context(nc.sbuf_tensor(name, shape, dt))

        def sem(name):
            return ctx.enter_context(nc.semaphore(name))

        agg = sb("agg", [P, 2, NP])
        xs = sb("xs", [P, NB, D])
        dst_tab = sb("dst_tab", [P, K, NCH])
        w_tab = sb("w_tab", [P, K, NCH])
        ring = sb("ring", [P, U, K * D])
        ef = sb("ef", [P, EF, K * DE])
        es = sb("es", [P, ES, K, DX])
        SS = sb("SS", [P, 3, K, P])
        S = SS[:, 0:2]
        SX = SS[:, 2]
        xrel = sb("xrel", [P, K])
        idx = sb("idx", [P, U, K], i32)
        MW = -(-(U + 1) // 4) * 4
        meta = sb("meta", [1, NM, MW], i32)
        ident = sb("ident", [P, P])
        w0_sb = sb("w0_sb", [P, D])
        w1_sb = sb("w1_sb", [P, D])
        wew = sb("wew", [P, D])
        b0_sb = sb("b0_sb", [P, D])
        b1_sb = sb("b1_sb", [P, D])
        pick = sb("pick", [P, 2])
        stage = sb("stage", [P, G, 2, P])
        stats = sb("stats", [P, G, 6])
        v = sb("v", [P, 2, G])
        r = sb("r", [P, 2, G])
        q = sb("q", [P, 2, G])
        scale = sb("scale", [P, G])
        shift = sb("shift", [P, G])
        dinv = sb("dinv", [P, NB])

        gbuf = sb("gbuf", [P, G, D])

        pre = SS[:, :, :, :].rearrange("p a k n -> p (a k n)")
        mn, mx, packed = pre[:, 0:5], pre[:, 5:10], pre[:, 10:15]
        span, extra = pre[:, 15:20].bitcast(i32), pre[:, 20:25].bitcast(i32)
        iota_i = pre[:, P:2 * P].bitcast(i32)
        we_sb = pre[0:DE, 2 * P:3 * P]
        weT = pre[:, 3 * P:3 * P + DE]
        packed_row = pre[0:1, 512:512 + NCH].bitcast(i32)
        least_row = pre[0:1, 512 + NCH:512 + 2 * NCH]
        least = [pre[0:1, 1296:1296 + NM + PAD], pre[0:1, 1296 + NM + PAD:1296 + 2 * (NM + PAD)]]
        group_i = pre[0:1, 448:448 + NM].bitcast(i32)
        group_s = pre[0:1, 25:25 + NM].bitcast(i32)
        ln = stage[:, :, :, :].rearrange("p g a n -> p (g a n)")
        stats0 = ln[:, 0:6 * NB].rearrange("p (b s) -> p b s", s=6)
        v0, r0, q0, u0, scale0, shift0 = (ln[:, (6 + n) * NB:(7 + n) * NB] for n in range(6))
        lx = ln[:, 12 * NB:12 * NB + 12 * U * K]
        stats_x = lx[:, 0:6 * U * K].rearrange("p (t s) -> p t s", s=6)
        vx, rx, qx, ux, scale_x, shift_x = (lx[:, (6 + n) * U * K:(7 + n) * U * K] for n in range(6))

        RL = 5 * CH
        assert 2 * RL <= NP
        rows_w = agg[:, 1, 0:RL].rearrange("p (g e) -> p g e", g=5)
        rows_d = agg[:, 1, RL:2 * RL].rearrange("p (g e) -> p g e", g=5)
        rows_di = agg[:, 1, RL:2 * RL].bitcast(i32).rearrange("p (g e) -> p g e", g=5)
        hbuf = agg[:, 0, 0:NB * P].rearrange("p (b d) -> p b d", d=D)

        bank = [ctx.enter_context(nc.psum_tensor(f"bank{i}", [P, 512], f32)) for i in range(8)]
        iota = bank[7][:, 0:P]
        win = [bank[0], bank[1]]
        winx = bank[2]
        tr = [bank[3], bank[4]]
        gt = [bank[5], bank[6]]

        ZB = [0, 0, 0, 1, 1, 2, 2]

        def z(j):
            at = j - ZB.index(ZB[j])
            return bank[3 + ZB[j]][:, at * D:(at + 1) * D]

        def z_last(j):
            return max(m for m in range(G) if ZB[m] == ZB[j]) + 1

        degs = bank[6][:, 0:2 * G].rearrange("p (g j) -> p g j", j=2)

        x_in = [sem(f"x_in{g}") for g in range(NBT)]
        rows_zero = sem("rows_zero")
        x_zero = sem("x_zero")
        rows_in = sem("rows_in")
        consts_in = sem("consts_in")
        ident_ok = sem("ident_ok")
        iota_ok = sem("iota_ok")
        wew_zero = sem("wew_zero")
        iota_ps = sem("iota_ps")
        rows_f = sem("rows_f")
        meta_t = sem("meta_t")
        tab_t = sem("tab_t")
        tab_ok = sem("tab_ok")
        dchain = sem("dchain")
        var_ok = sem("var_ok")
        sqrt_ok = sem("sqrt_ok")
        affine_ok = sem("affine_ok")
        h_ready = sem("h_ready")
        h_out = [sem(f"h_out{g}") for g in range(NBT)]
        agg_zero = sem("agg_zero")
        we_t = sem("we_t")
        we_tc = sem("we_tc")
        wew_t = sem("wew_t")
        wew_ok = sem("wew_ok")
        es_ones = sem("es_ones")
        ef_in = [sem(f"ef_in{i}") for i in range(EF)]
        es_ready = sem("es_ready")

        class Layer:

            def __init__(self, n):
                self.idx_in = [sem(f"idx_in{n}_{h}") for h in range(2)]
                self.opened = sem(f"opened{n}")
                self.got = [sem(f"got{n}_{u}") for u in range(U)]
                self.s_ready = sem(f"s_ready{n}")
                self.win_ready = sem(f"win_ready{n}")
                self.added = sem(f"added{n}")
                self.xrel_ok = sem(f"xrel_ok{n}")
                self.sx_ready = sem(f"sx_ready{n}")
                self.winx_ready = sem(f"winx_ready{n}")
                self.addedx = sem(f"addedx{n}")

        L0, L1 = Layer(0), Layer(1)
        hp_affine = sem("hp_affine")
        hp_ready = sem("hp_ready")
        vx_ok = sem("vx_ok")
        sqrt_x_ok = sem("sqrt_x_ok")
        affine_x_ok = sem("affine_x_ok")
        normed = sem("normed")
        stx_ok = sem("stx_ok")
        rows_d_ok = sem("rows_d_ok")
        mn_ok = sem("mn_ok")
        st_ok = sem("st_ok")
        last_open = sem("last_open")
        final_ok = sem("final_ok")
        pick_ok = sem("pick_ok")
        staged = sem("staged")
        deg_t = sem("deg_t")
        gvar_ok = sem("gvar_ok")
        gsqrt_ok = sem("gsqrt_ok")
        z_ready = sem("z_ready")
        t_ok = sem("t_ok")
        x1_ok = sem("x1_ok")
        gst_ok = sem("gst_ok")
        gchain = sem("gchain")
        gaffine_ok = sem("gaffine_ok")
        g_ready = sem("g_ready")
        g_ready2 = sem("g_ready2")
        g_out = sem("g_out")
        g_t = sem("g_t")
        seeded = sem("seeded")
        staged1 = sem("staged1")
        z1_ready = sem("z1_ready")
        t1_ok = sem("t1_ok")
        out_ok = sem("out_ok")
        out_done = sem("out_done")

        block = ctx.enter_context(nc.Block())

        def batch(a, g):
            return a[:, CUTS[g]:CUTS[g + 1]]

        def half(a, h):
            return a[:, h * HT:(h + 1) * HT]

        def loop(eng, n, body, first=1):
            for i in range(first):
                body(i)
            with eng.Fori(first, n) as i:
                body(i)

        def ge(eng, s, val):
            if not (isinstance(val, int) and val <= 0):
                eng.wait_ge(s, val)

        def load_meta(eng, regs, i):
            eng.load(regs, meta[0:1, bass.ds(i, 1), U + 1 - len(regs):U + 1])

        def next_words(eng, words, last, i):
            eng.reg_mov(last[0], words[U - 1])
            eng.reg_mov(last[1], words[U])
            load_meta(eng, words, i + 1)

        def node_groups(eng, i, count, grp, work):
            if isinstance(i, int) and i == 0:
                return
            n = eng.snap(count, min_val=0, max_val=NG)
            with eng.If(n > 0):
                with eng.Fori(0, n):
                    work()
                    eng.reg_add(grp, grp, 1)
            with eng.Else():
                pass

        xg = x[0:(NB - 1) * P, :].rearrange("(b p) d -> p b d", p=P)
        og = out[0:(NB - 1) * P, :].rearrange("(b p) d -> p b d", p=P)
        hg = h_tab.rearrange("(b p) d -> p b d", p=P)
        gg = g_tab.rearrange("(b p) d -> p b d", p=P)

        @block.sync
        def _(sp):
            def load_idx(L, i, h, used):
                for u in range(h * HU, (h + 1) * HU):
                    for s, n in used(u):
                        ge(sp, s, n)
                sp.dma_start(idx[:, h * HU:(h + 1) * HU, :],
                             src[bass.ds((i * U + h * HU) * CH, HU * CH)]
                             .rearrange("(u p k) -> p u k", u=HU, k=K)).then_inc(L.idx_in[h], 16)

            def load_idx_tail(L):
                sp.wait_ge(L.got[0], 16 * K * IT)
                sp.dma_start(idx[0:TP, 0, :], src[NC * CH:E].rearrange("(p k) -> p k", k=K)
                             ).then_inc(L.idx_in[0], 16)

            for h in range(2):
                load_idx(L0, 0, h, lambda u: [])
            for g in range(NBT):
                lo, hi = CUTS[g], min(CUTS[g + 1], NB - 1)
                sp.dma_start(xs[:, lo:hi, :], xg[:, lo:hi, :]).then_inc(x_in[g], 16)
            sp.wait_ge(x_zero, 1)
            sp.dma_start(xs[0:NT, NB - 1, :], x[(NB - 1) * P:N, :]).then_inc(x_in[NBT - 1], 16)
            sp.dma_start(w0_sb[:, :], w0).then_inc(consts_in, 16)
            sp.dma_start(w1_sb[:, :], w1).then_inc(consts_in, 16)
            sp.dma_start(we_sb, w0_edge).then_inc(consts_in, 16)
            sp.dma_start(b0_sb[:, :], b0.partition_broadcast(P)).then_inc(consts_in, 16)
            sp.dma_start(b1_sb[:, :], b1.partition_broadcast(P)).then_inc(consts_in, 16)

            def ef_load(c, u):
                ge(sp, es_ready, 2 * (c - EF + 1))
                sp.dma_start(ef[:, u % EF, :], edge_attr[bass.ds(c * CH, CH), :]
                             .rearrange("(p k) d -> p (k d)", k=K)).then_inc(ef_in[u % EF], 16)

            for u in range(EF):
                ef_load(u, u)
            for g in range(NBT):
                lo, hi = CUTS[g], CUTS[g + 1]
                sp.wait_ge(h_ready, hi if g < NBT - 1 else NB - PB)
                if g == NBT - 1:
                    sp.wait_ge(hp_ready, 1)
                sp.dma_start(hg[:, lo:hi, :], hbuf[:, lo:hi, :]).then_inc(h_out[g], 16)

            for h in range(2):
                load_idx(L0, 1, h, lambda u: [(L0.got[u], 16 * K)])
            for c in range(EF, U + IL):
                ef_load(c, c % U)

            with sp.Fori(2, IT) as i:
                load_idx(L0, i, 0, lambda u: [(L0.got[u], 16 * K * i)])
                for u in range(IL, U):
                    ef_load((i - 1) * U + u, u)
                for u in range(IL - HU + 1):
                    ef_load(i * U + u, u)
                load_idx(L0, i, 1, lambda u: [(L0.got[u], 16 * K * i)])
                for u in range(IL - HU + 1, IL):
                    ef_load(i * U + u, u)

            load_idx_tail(L0)
            for u in range(IL, U):
                ef_load((IT - 1) * U + u, u)
            sp.wait_ge(es_ready, 2 * (NC - EF + 1))
            sp.dma_start(ef[0:TP, 0, :], edge_attr[NC * CH:E, :].rearrange("(p k) d -> p (k d)", k=K)
                         ).then_inc(ef_in[0], 16)

            def body1(i):
                for h in range(2):
                    if isinstance(i, int):
                        load_idx(L1, i, h, lambda u: [(L0.got[u], 16 * K * (IT + (u == 0)))])
                    else:
                        load_idx(L1, i, h, lambda u: [(L1.got[u], 16 * K * i)])

            loop(sp, IT, body1)
            load_idx_tail(L1)

        @block.gpsimd
        def _(pool):
            pool.memset(xs[:, NB - 1, :], 0.0).then_inc(x_zero, 1)
            for rows in (rows_di, rows_w):
                pool.memset(rows[:, RG:RG + 2, :], 0).then_inc(rows_zero, 1)
            pool.memset(ident[:, :], 0.0).then_inc(ident_ok, 1)
            pool.wait_ge(ident_ok, 1)
            pool.affine_select(out=ident[:, :], in_=ident[:, :], compare_op=ALU.not_equal, fill=1.0,
                               base=0, pattern=[[-1, P]], channel_multiplier=1).then_inc(ident_ok, 1)
            pool.iota(iota_i, pattern=[[1, P]], base=0, channel_multiplier=0).then_inc(iota_ok, 1)
            pool.memset(es[:, :, :, :], 1.0).then_inc(es_ones, 1)
            pool.memset(wew[:, :], 0.0).then_inc(wew_zero, 1)
            pool.memset(pick[:, :], 0.0).then_inc(pick_ok, 1)
            pool.wait_ge(pick_ok, 1)
            pool.affine_select(out=pick[:, :], in_=pick[:, :], compare_op=ALU.not_equal, fill=1.0,
                               base=-DE, pattern=[[-1, 2]], channel_multiplier=1).then_inc(pick_ok, 1)

            def gathers(L, table, i, u, rows, added):
                c = i * U + u
                if u % HU == 0:
                    pool.wait_ge(L.idx_in[u // HU], 16 * (i + 1))
                ge(pool, L.added, added * (c - U + 1))
                pool.sem_inc(L.opened, 1)
                for k in range(K):
                    pool.indirect_dma_start(
                        ring[0:rows, u, k * D:(k + 1) * D], None, table[:, :],
                        bass.IndirectOffsetOnAxis(ap=idx[0:rows, u, k:k + 1], axis=0),
                    ).then_inc(L.got[u], 16)

            pool.sem_inc(g_out, 16)
            for u in range(U):
                gathers(L0, x, 0, u, P, 2)
            def zero_batch(g):
                pool.wait_ge(h_out[g], 16)
                pool.memset(agg[:, 0, CUTS[g] * P:CUTS[g + 1] * P], 0.0).then_inc(agg_zero, 1)

            for g in range(NBT - 2):
                zero_batch(g)
            pool.wait_ge(affine_ok, NBT)
            for b in range(NB - PB, NB):
                pool.tensor_scalar(hbuf[:, b, :], xs[:, b, :], scale0[:, b:b + 1], shift0[:, b:b + 1],
                                   ALU.mult, ALU.add).then_inc(hp_affine, 1)
            pool.wait_ge(hp_affine, PB)
            pool.tensor_scalar(hbuf[:, NB - PB:NB, :], hbuf[:, NB - PB:NB, :], 0.0, None, ALU.max
                               ).then_inc(hp_ready, 1)
            pool.wait_ge(tab_t, 2 * K)
            pool.memset(agg[:, 1, :], 0.0).then_inc(agg_zero, 1)
            zero_batch(NBT - 1)

            for L, table, done, first, added in ((L0, h_tab, [(h_out[NBT - 2], 16)], 1, 2),
                                                 (L1, g_tab, [(g_out, 16 * (NG + 1))], 0, 1)):
                for s, n in done:
                    pool.wait_ge(s, n)
                def body(i):
                    for u in range(U):
                        gathers(L, table, i, u, P, added)

                if first == 0:
                    body(0)
                with pool.Fori(1, IT) as i:
                    body(i)
                gathers(L, table, IT, 0, TP, added)

        @block.scalar
        def _(act):
            def norm_rows(g, blocks):
                act.wait_ge(affine_ok, g + 1)
                for b in blocks:
                    act.activation(hbuf[:, bass.ds(b, 1), :], xs[:, bass.ds(b, 1), :], ACT.Relu,
                                   bias=shift0[:, bass.ds(b, 1)], scale=scale0[:, bass.ds(b, 1)]
                                   ).then_inc(h_ready, 1)

            def table(n):
                act.wait_ge(tab_t, n + 1)
                act.activation((dst_tab, w_tab)[n // K][:, n % K, :], tr[n % 2][:, 0:NCH], ACT.Copy
                               ).then_inc(tab_ok, 1)

            act.wait_ge(rows_zero, 2)
            for i, (rows, a) in enumerate(((rows_di, dst), (rows_w, edge_w))):
                act.dma_start(rows[:, 0:RG, :], a[0:RG * P * CH].rearrange("(g c e) -> c g e", g=RG, c=P)
                              ).then_inc(rows_in, 16)
                act.dma_start(rows[0:RR, RG, :], a[RG * P * CH:NC * CH].rearrange("(c e) -> c e", c=RR)
                              ).then_inc(rows_in, 16)
                act.dma_start(rows[0:1, RG + 1, 0:TAIL], a[NC * CH:E].rearrange("(c e) -> c e", c=1)
                              ).then_inc(rows_in, 16)
                act.dma_start(rows[0:1, RG + 1, TAIL:CH], a[E - CH + TAIL:E].rearrange("(c e) -> c e", c=1)
                              ).then_inc(rows_in, 16)
            def sqrt0(g):
                act.wait_ge(var_ok, g + 1)
                act.activation(batch(q0, g), batch(v0, g), ACT.Sqrt).then_inc(sqrt_ok, 1)

            sqrt0(0)
            for g in range(1, NBT - 1):
                sqrt0(g)
                norm_rows(g - 1, range(CUTS[g - 1], CUTS[g]))
            blocks = range(CUTS[NBT - 2], CUTS[NBT - 1])
            head = len(blocks) - 2 * K * LB
            norm_rows(NBT - 2, blocks[0:head])
            sqrt0(NBT - 1)
            for n in range(2 * K):
                table(n)
                norm_rows(NBT - 2, blocks[head + n * LB:head + (n + 1) * LB])
            act.wait_ge(vx_ok, 1)
            act.activation(half(qx, 0), half(vx, 0), ACT.Sqrt).then_inc(sqrt_x_ok, 1)
            norm_rows(NBT - 1, range(CUTS[NBT - 1], NB - PB))
            act.wait_ge(we_t, 1)
            act.activation(weT, gt[0][:, 0:DE], ACT.Copy).then_inc(we_tc, 1)
            act.wait_ge(wew_t, 1)
            act.wait_ge(wew_zero, 1)
            act.activation(wew[0:DE, :], gt[1][0:DE, 0:D], ACT.Copy).then_inc(wew_ok, 1)
            def edge_cols(i, u):
                c = i * U + u
                ge(act, L0.added, 2 * (c - ES + 1))
                act.wait_ge(ef_in[u % EF], 16 * (i * (U // EF) + u // EF + 1))
                act.activation(es[:, u % ES, :, 0:DE], ef[:, u % EF, :].rearrange("p (k d) -> p k d", k=K),
                               ACT.Copy).then_inc(es_ready, 1)
                act.activation(es[:, u % ES, :, DE + 1:DX], w_tab[:, :, bass.ds(c, 1)], ACT.Copy
                               ).then_inc(es_ready, 1)

            def tail_cols():
                act.wait_ge(L0.added, 2 * (NC - ES + 1))
                act.wait_ge(ef_in[0], 16 * (IT * (U // EF) + 1))
                act.activation(es[0:TP, 0, :, 0:DE], ef[0:TP, 0, :].rearrange("p (k d) -> p k d", k=K),
                               ACT.Copy).then_inc(es_ready, 1)
                act.activation(es[0:TP, 0, :, DE + 1:DX], w_tab[0:TP, :, NC:NC + 1], ACT.Copy
                               ).then_inc(es_ready, 1)

            grp = act.alloc_register("act_group")
            count = act.alloc_register("act_final_groups")

            def node_group0(added):
                g = act.snap(grp, min_val=0, max_val=NG - 1)
                act.wait_ge(L0.added, added)
                for j in range(G):
                    act.activation(stage[:, j, :, :], agg[:, :, bass.ds((g * G + j) * P, P)], ACT.Copy
                                   ).then_inc(staged, 1)
                for n in range(2):
                    act.wait_ge(gvar_ok, g * 2 + (n + 1))
                    w = 2 - n
                    act.activation(q[:, 0:w, :], v[:, 0:w, :], ACT.Sqrt).then_inc(gsqrt_ok, 1)
                act.wait_ge(gaffine_ok, g + 1)
                for j in range(G4):
                    act.activation(gbuf[:, j:j + 1, :], xs[:, bass.ds(g * G + j, 1), :], ACT.Relu,
                                   bias=shift[:, j:j + 1], scale=scale[:, j:j + 1]).then_inc(g_ready, 1)
                act.wait_ge(g_ready, (g + 1) * G4)
                act.wait_ge(g_ready2, g + 1)
                act.dma_start(gg[:, bass.ds(g * G, G), :], gbuf[:, :, :]).then_inc(g_out, 16)

            def node_group1(added):
                g = act.snap(grp, min_val=0, max_val=NG - 1)
                act.wait_ge(L1.added, added)
                for j in range(G):
                    act.activation(stage[:, j, 0, :], agg[:, 0, bass.ds((g * G + j) * P, P)], ACT.Copy
                                   ).then_inc(staged1, 1)
                with act.If(g < NG - 1):
                    g = act.snap(grp, min_val=0, max_val=NG - 2)
                    act.wait_ge(out_ok, (g + 1) * G)
                    act.dma_start(og[:, bass.ds(g * G, G), :], xs[:, bass.ds(g * G, G), :]).then_inc(out_done, 16)
                with act.Else():
                    act.wait_ge(out_ok, NB)
                    act.dma_start(og[:, NB - G:NB - 1, :], xs[:, NB - G:NB - 1, :]).then_inc(out_done, 16)
                    act.dma_start(out[(NB - 1) * P:N, :], xs[0:NT, NB - 1, :]).then_inc(out_done, 16)

            act.wait_ge(tab_ok, 2 * K)
            act.wait_ge(es_ones, 1)
            for u in range(U):
                if u % HU == 0:
                    act.wait_ge(affine_x_ok, u // HU + 1)
                if u == 1:
                    act.wait_ge(vx_ok, 2)
                    act.activation(half(qx, 1), half(vx, 1), ACT.Sqrt).then_inc(sqrt_x_ok, 1)
                for k in range(K):
                    t = u * K + k
                    row = ring[:, u, k * D:(k + 1) * D]
                    act.activation(row, row, ACT.Relu, bias=shift_x[:, t:t + 1], scale=scale_x[:, t:t + 1]
                                   ).then_inc(normed, 1)
                if u < ES:
                    edge_cols(0, u)
                elif u > ES:
                    edge_cols(0, u - 1)
            edge_cols(0, U - 1)

            for L, adds, node_group in ((L0, 2, node_group0), (L1, 1, node_group1)):
                act.reg_mov(grp, 0)
                def body(i):
                    if L is L0 and not isinstance(i, int):
                        for u in range(U):
                            edge_cols(i, u)
                    load_meta(act, [count], i)
                    node_groups(act, i, count, grp, lambda: node_group(adds * U * (i + 1)))

                if L is L0:
                    act.wait_ge(final_ok, 1)
                loop(act, IT, body)
                if L is L0:
                    tail_cols()
                load_meta(act, [count], IT)
                node_groups(act, IT, count, grp, lambda: node_group(adds * NCH))
            act.wait_ge(out_done, (NG + 1) * 16)

        @block.vector
        def _(dve):
            links = [0]

            def link(ins):
                links[0] += 1
                ins.then_inc(dchain, 1)
                dve.wait_ge(dchain, links[0])

            def variance(lk, st, vv, mean2, a, b):
                nc.vector.tensor_tensor(mean2, st[:, :, 1], st[:, :, 4], ALU.add)
                nc.vector.tensor_tensor(a, st[:, :, 1], st[:, :, 4], ALU.subtract)
                lk(nc.vector.tensor_tensor(b, st[:, :, 2], st[:, :, 5], ALU.add))
                nc.vector.tensor_scalar(b, b, 1.0 / D, EPS, ALU.mult, ALU.add)
                lk(nc.vector.tensor_tensor(a, a, a, ALU.mult))
                return nc.vector.scalar_tensor_tensor(out=vv, in0=a, scalar=0.25, in1=b,
                                                      op0=ALU.mult, op1=ALU.add)

            def rsqrt(lk, vv, rr, qq):
                lk(nc.vector.reciprocal(rr, qq))
                lk(nc.vector.tensor_tensor(qq, rr, rr, ALU.mult))
                lk(nc.vector.tensor_tensor(qq, qq, vv, ALU.mult))
                lk(nc.vector.tensor_scalar(qq, qq, -0.5, 1.5, ALU.mult, ALU.add))
                lk(nc.vector.tensor_tensor(rr, rr, qq, ALU.mult))

            def windows():
                dve.wait_ge(rows_in, 8 * 16)
                link(nc.vector.tensor_copy(rows_d, rows_di))
                nc.vector.tensor_reduce(mn, rows_d, AX.X, ALU.min)
                link(nc.vector.tensor_reduce(mx, rows_d, AX.X, ALU.max))
                nc.vector.tensor_tensor(span, mx, mn, ALU.subtract).then_inc(mn_ok, 1)
                dve.wait_ge(mn_ok, 1)
                link(nc.vector.tensor_scalar(extra, span, 7, None, ALU.arith_shift_right))
                nc.vector.scalar_tensor_tensor(out=packed, in0=mn, scalar=float(P), in1=extra,
                                               op0=ALU.mult, op1=ALU.add).then_inc(rows_f, 1)
                for g in range(5):
                    nc.vector.tensor_scalar(rows_d[:, g, :], rows_d[:, g, :], mn[:, g:g + 1], None, ALU.subtract
                                            ).then_inc(rows_d_ok, 1)
                dve.wait_ge(iota_ok, 1)
                nc.vector.tensor_copy(iota, iota_i).then_inc(iota_ps, 1)

            def least_dst():
                dve.wait_ge(meta_t, 1)
                link(nc.vector.tensor_copy(packed_row, gt[0][0:1, 0:NCH]))
                link(nc.vector.tensor_scalar(least_row.bitcast(i32), packed_row, 7, None, ALU.arith_shift_right))
                nc.vector.memset(meta[:, :, :], 0)
                nc.vector.memset(least[0], float(NB * P))
                link(nc.vector.memset(least[1], float(NB * P)))
                nc.vector.tensor_copy(meta[:, 0:IT, 0:U], packed_row[:, 0:NC].rearrange("o (i u) -> o i u", u=U))
                nc.vector.tensor_copy(meta[:, IT, 0:1], packed_row[:, NC:NCH])
                nc.vector.tensor_reduce(least[0][:, 0:IT - 1], least_row.bitcast(i32)[:, U:NC]
                                        .rearrange("o (i u) -> o i u", u=U), AX.X, ALU.min)
                link(nc.vector.tensor_copy(least[0][:, IT - 1:IT], least_row.bitcast(i32)[:, NC:NCH]))
                n, reach = 0, 1
                while reach < NM:
                    link(nc.vector.tensor_tensor(least[1 - n][:, 0:NM], least[n][:, 0:NM],
                                                 least[n][:, reach:reach + NM], ALU.min))
                    n, reach = 1 - n, 2 * reach
                link(nc.vector.tensor_copy(group_i, least[n][:, 0:NM]))
                link(nc.vector.tensor_scalar(group_s, group_i, 7, None, ALU.arith_shift_right))
                link(nc.vector.tensor_scalar(group_i, group_s, 147.0, None, ALU.mult))
                link(nc.vector.tensor_scalar(group_s, group_i, 10, None, ALU.arith_shift_right))
                link(nc.vector.tensor_copy(meta[:, 0:2, U], group_s[:, 0:2]))
                nc.vector.tensor_tensor(meta[:, 2:NM, U], group_s[:, 2:NM], group_s[:, 1:NM - 1], ALU.subtract
                                        ).then_inc(final_ok, 1)

            def affine0(g):
                dve.wait_ge(sqrt_ok, g + 1)
                rr = batch(r0, g)
                rsqrt(link, batch(v0, g), rr, batch(q0, g))
                nc.vector.tensor_copy(batch(scale0, g), rr)
                nc.vector.scalar_tensor_tensor(out=batch(shift0, g), in0=batch(u0, g), scalar=-0.5, in1=rr,
                                               op0=ALU.mult, op1=ALU.mult).then_inc(affine_ok, 1)

            def ring_norm(h):
                for t in range(h * HT, (h + 1) * HT):
                    if t % K == 0:
                        dve.wait_ge(L0.got[t // K], 16 * K)
                    nc.vector.bn_stats(stats_x[:, t, :], ring[:, t // K, t % K * D:(t % K + 1) * D]
                                       ).then_inc(stx_ok, 1)
                dve.wait_ge(stx_ok, (h + 1) * HT)
                variance(link, stats_x[:, h * HT:(h + 1) * HT, :], half(vx, h), half(ux, h), half(rx, h),
                         half(shift_x, h)).then_inc(vx_ok, 1)

            def ring_affine(h):
                dve.wait_ge(sqrt_x_ok, h + 1)
                rsqrt(link, half(vx, h), half(rx, h), half(qx, h))
                nc.vector.tensor_copy(half(scale_x, h), half(rx, h))
                nc.vector.scalar_tensor_tensor(out=half(shift_x, h), in0=half(ux, h), scalar=-0.5,
                                               in1=half(rx, h), op0=ALU.mult, op1=ALU.mult
                                               ).then_inc(affine_x_ok, 1)

            for g in range(NBT):
                dve.wait_ge(x_in[g], 16 if g < NBT - 1 else 32)
                for b in range(CUTS[g], CUTS[g + 1]):
                    dve.bn_stats(stats0[:, bass.ds(b, 1), :].rearrange("p o s -> p (o s)"),
                                 xs[:, bass.ds(b, 1), :].rearrange("p o d -> p (o d)")).then_inc(st_ok, 1)
                if 0 < g < NBT - 1:
                    affine0(g - 1)
                dve.wait_ge(st_ok, CUTS[g + 1])
                variance(link, stats0[:, CUTS[g]:CUTS[g + 1], :], batch(v0, g), batch(u0, g), batch(r0, g),
                         batch(shift0, g)).then_inc(var_ok, 1)
                if g == NBT - 2:
                    affine0(g)
                    windows()
            ring_norm(0)
            affine0(NBT - 1)

            least_dst()
            nc.vector.memset(agg[:, 0, NB * P:NP], 0.0).then_inc(agg_zero, 1)
            ring_affine(0)
            ring_norm(1)
            dve.wait_ge(h_out[NBT - 2], 16)
            nc.vector.memset(agg[:, 0, CUTS[NBT - 2] * P:CUTS[NBT - 1] * P], 0.0).then_inc(agg_zero, 1)
            ring_affine(1)

            extras = dve.alloc_register("extras_seen")
            writes = dve.alloc_register("xrel_writes")
            start = dve.alloc_register("window_start")
            startx = dve.alloc_register("extra_window_start")

            def one_hot(L, dest, rel):
                for k in range(K):
                    d, w = rel(k)
                    if L is L0:
                        last = nc.vector.tensor_scalar(dest[:, k, :], iota, d, None, ALU.is_equal)
                    else:
                        last = nc.vector.tensor_scalar(dest[:, k, :], iota, d, w, ALU.is_equal, ALU.mult)
                return last

            def add_window(L, at, ps, s):
                ops = [(D, 0)] if L is L1 else [(D, 0), (DX, 1)]
                for rows, plane in ops:
                    w = agg[0:rows, plane, bass.ds(at, P)]
                    nc.vector.tensor_tensor(w, w, ps[0:rows, plane * P:(plane + 1) * P], ALU.add).then_inc(s, 1)

            def build(L, c, u):
                ge(dve, L.win_ready, c - 1)
                col = bass.ds(c, 1)
                one_hot(L, S[:, u % 2], lambda k: (dst_tab[:, k, col], w_tab[:, k, col])).then_inc(L.s_ready, 1)

            def finish(L, c, u, packed_c):
                adds = 2 if L is L0 else 1
                n = packed_c & (P - 1)
                dve.reg_mov(start, packed_c >> 7)
                at = dve.snap(start, min_val=0, max_val=N - 1)
                ge(dve, L.added, adds * c)
                col = bass.ds(c, 1)
                with dve.If(n > 0):
                    nc.vector.tensor_copy(xrel[:, :], dst_tab[:, :, col].rearrange("p k o -> p (k o)")
                                          ).then_inc(L.xrel_ok, 1)
                    dve.reg_add(writes, writes, 1)
                    dve.reg_mov(startx, start)
                    with dve.Fori(0, n):
                        dve.wait_ge(L.xrel_ok, dve.snap(writes, min_val=1))
                        nc.vector.tensor_scalar(xrel[:, :], xrel[:, :], float(-P), None, ALU.add
                                                ).then_inc(L.xrel_ok, 1)
                        dve.reg_add(writes, writes, 1)
                        dve.reg_add(extras, extras, 1)
                        dve.reg_add(startx, startx, P)
                        dve.wait_ge(L.xrel_ok, dve.snap(writes, min_val=1))
                        one_hot(L, SX, lambda k: (xrel[:, k:k + 1], w_tab[:, k, col])).then_inc(L.sx_ready, 1)
                        dve.wait_ge(L.winx_ready, dve.snap(extras, min_val=1))
                        add_window(L, dve.snap(startx, min_val=0, max_val=N - 1), winx, L.addedx)
                with dve.Else():
                    pass
                dve.wait_ge(L.win_ready, c + 1)
                add_window(L, at, win[u % 2], L.added)

            LINKS = 17

            def node_group0():
                g = dve.snap(grp, min_val=0, max_val=NG - 1)
                steps = [0]

                def glink(ins):
                    steps[0] += 1
                    ins.then_inc(gchain, 1)
                    dve.wait_ge(gchain, g * LINKS + steps[0])

                dve.wait_ge(deg_t, g + 1)
                glink(nc.vector.tensor_scalar(r[:, 1, :], degs[:, :, 1], 1.0, None, ALU.add))
                nc.vector.tensor_scalar(v[:, 0, :], degs[:, :, 0], 1.0, None, ALU.max)
                nc.vector.tensor_scalar(v[:, 1, :], r[:, 1, :], 1e-30, None, ALU.max).then_inc(gvar_ok, 1)
                glink(nc.vector.tensor_scalar(scale[:, :], r[:, 1, :], 0.0, None, ALU.is_gt))
                dve.wait_ge(gsqrt_ok, g * 2 + 1)
                rsqrt(glink, v[:, :, :], r[:, :, :], q[:, :, :])
                glink(nc.vector.tensor_tensor(dinv[:, bass.ds(g * G, G)], r[:, 1, :], scale[:, :], ALU.mult))
                dve.wait_ge(g_out, g * 16 + 16)
                for j in range(G + 2):
                    if j - 2 >= 0:
                        dve.wait_ge(x1_ok, g * G + (j - 1))
                    if j < G:
                        dve.wait_ge(z_ready, g * G + z_last(j))
                        nc.vector.scalar_tensor_tensor(out=gbuf[:, j, :], in0=z(j), scalar=r[:, 0, j:j + 1],
                                                       in1=b0_sb[:, :], op0=ALU.mult, op1=ALU.add
                                                       ).then_inc(t_ok, 1)
                    if 0 <= j - 1 < G:
                        relu_add(g, j - 1, t_ok, x1_ok)
                    if j == G + 1:
                        dve.sem_inc(last_open, 1)
                    if j - 2 >= 0:
                        nc.vector.bn_stats(stats[:, j - 2, :], xs[:, bass.ds(g * G + (j - 2), 1), :]
                                           .rearrange("p o d -> p (o d)")).then_inc(gst_ok, 1)
                dve.wait_ge(gst_ok, (g + 1) * G)
                variance(glink, stats[:, :, :], v[:, 0, :], r[:, 1, :], r[:, 0, :], v[:, 1, :]
                         ).then_inc(gvar_ok, 1)
                dve.wait_ge(gsqrt_ok, g * 2 + 2)
                rsqrt(glink, v[:, 0, :], r[:, 0, :], q[:, 0, :])
                glink(nc.vector.tensor_tensor(scale[:, :], r[:, 0, :], dinv[:, bass.ds(g * G, G)], ALU.mult))
                nc.vector.scalar_tensor_tensor(out=shift[:, :], in0=r[:, 1, :], scalar=-0.5, in1=scale[:, :],
                                               op0=ALU.mult, op1=ALU.mult).then_inc(gaffine_ok, 1)
                dve.wait_ge(gaffine_ok, g + 1)
                for j in range(G4, G):
                    last = nc.vector.tensor_scalar(gbuf[:, j, :], xs[:, bass.ds(g * G + j, 1), :]
                                                   .rearrange("p o d -> p (o d)"), scale[:, j:j + 1],
                                                   shift[:, j:j + 1], ALU.mult, ALU.add)
                glink(last)
                nc.vector.tensor_scalar(gbuf[:, G4:G, :], gbuf[:, G4:G, :], 0.0, None, ALU.max
                                        ).then_inc(g_ready2, 1)
                for n, w in ((0, G4), (1, G - G4)):
                    dve.wait_ge(g_t, g * G + (n * G4 + w))
                    nc.vector.tensor_copy(agg[:, 0, bass.ds((g * G + n * G4) * P, w * P)], gt[n][:, 0:w * P]
                                          ).then_inc(seeded, 1)
                assert steps[0] == LINKS, steps[0]

            def relu_add(g, j, ts, done):
                dve.wait_ge(ts, g * G + (j + 1))
                xb = xs[:, bass.ds(g * G + j, 1), :].rearrange("p o d -> p (o d)")
                nc.vector.scalar_tensor_tensor(out=xb, in0=gbuf[:, j, :], scalar=0.0, in1=xb,
                                               op0=ALU.max, op1=ALU.add).then_inc(done, 1)

            def node_group1():
                g = dve.snap(grp, min_val=0, max_val=NG - 1)
                for j in range(G + 1):
                    if j < G:
                        dve.wait_ge(z1_ready, g * G + z_last(j))
                        nc.vector.scalar_tensor_tensor(out=gbuf[:, j, :], in0=z(j),
                                                       scalar=dinv[:, bass.ds(g * G + j, 1)],
                                                       in1=b1_sb[:, :], op0=ALU.mult, op1=ALU.add
                                                       ).then_inc(t1_ok, 1)
                    if j > 0:
                        relu_add(g, j - 1, t1_ok, out_ok)
                dve.wait_ge(out_ok, (g + 1) * G)

            grp = dve.alloc_register("dve_group")
            words = [dve.alloc_register(f"dve_meta{u}") for u in range(U + 1)]
            last = [dve.alloc_register(f"dve_last{n}") for n in range(2)]

            def edge_loop(L, node_group):
                dve.reg_mov(extras, 0)
                dve.reg_mov(writes, 0)
                dve.reg_mov(grp, 0)

                def body(i):
                    for u in range(U):
                        build(L, i * U + u + 1, u + 1)
                        if u == U - 1:
                            next_words(dve, words, last, i)
                        finish(L, i * U + u, u, dve.snap(words[u] if u < U - 1 else last[0],
                                                         min_val=0, max_val=N * P))
                    node_groups(dve, i, last[1], grp, node_group)

                load_meta(dve, words, 0)
                build(L, 0, 0)
                loop(dve, IT, body)
                finish(L, NC, 0, dve.snap(words[0], min_val=0, max_val=N * P))
                node_groups(dve, IT, words[U], grp, node_group)

            dve.wait_ge(consts_in, 5 * 16)
            dve.wait_ge(final_ok, 1)
            dve.wait_ge(tab_ok, 2 * K)
            dve.wait_ge(wew_ok, 1)
            dve.wait_ge(iota_ps, 1)
            dve.wait_ge(agg_zero, NBT + 2)
            dve.sem_inc(seeded, 2)
            edge_loop(L0, node_group0)
            dve.wait_ge(seeded, 2 * (NG + 1))
            edge_loop(L1, node_group1)

        @block.tensor
        def _(pe):
            mm = nc.tensor.matmul
            pe.wait_ge(ident_ok, 2)
            pe.wait_ge(rows_f, 1)
            groups = [(g, P) for g in range(RG)] + [(RG, RR), (RG + 1, 1)]
            place = [0, P, 2 * P, RG * P, NC]
            for g, n in groups:
                last = nc.tensor.transpose(gt[0][0:1, place[g]:place[g] + n], packed[0:n, g:g + 1],
                                           ident[0:n, 0:n])
            last.then_inc(meta_t, 1)
            for n in range(2 * K):
                rows, k = (rows_d, rows_w)[n // K], n % K
                ge(pe, tab_ok, n - 1)
                if n == 0:
                    pe.wait_ge(rows_d_ok, 5)
                for g, m in groups:
                    last = nc.tensor.transpose(tr[n % 2][:, place[g]:place[g] + m],
                                               rows[0:m, g, :].rearrange("c (p k) -> c k p", k=K)[:, k, :],
                                               ident[0:m, 0:m])
                last.then_inc(tab_t, 1)
            pe.wait_ge(consts_in, 5 * 16)
            pe.wait_ge(final_ok, 1)
            nc.tensor.transpose(gt[0][:, 0:DE], we_sb, ident[0:DE, 0:DE]).then_inc(we_t, 1)
            pe.wait_ge(we_tc, 1)
            mm(gt[1][0:DE, 0:D], weT, w0_sb[:, :], start=True, stop=True).then_inc(wew_t, 1)

            extras = pe.alloc_register("extras_done")

            def sums(L, ps, slot, ti, tiles, rows, s):
                for k in range(K):
                    last = mm(ps[:, 0:P], ring[0:rows, slot, k * D:(k + 1) * D], tiles[0:rows, k, :],
                              start=(k == 0), stop=(k == K - 1))
                if L is L0:
                    for k in range(K):
                        last = mm(ps[0:DX, P:2 * P], es[0:rows, ti, k, :], tiles[0:rows, k, :],
                                  start=(k == 0), stop=(k == K - 1))
                last.then_inc(s, 1)

            def chunk(L, c, u, rows, fills, val):
                n = val & (P - 1)
                if L is L0 and isinstance(c, int) and c < U:
                    pe.wait_ge(normed, K * (c + 1))
                else:
                    pe.wait_ge(L.got[u], 16 * K * fills)
                if L is L0:
                    pe.wait_ge(es_ready, 2 * (c + 1))
                pe.wait_ge(L.s_ready, c + 1)
                ge(pe, L.added, (2 if L is L0 else 1) * (c - 1))
                sums(L, win[u % 2], u, u % ES, S[:, u % 2], rows, L.win_ready)
                with pe.If(n > 0):
                    with pe.Fori(0, n):
                        pe.reg_add(extras, extras, 1)
                        pe.wait_ge(L.sx_ready, pe.snap(extras, min_val=1))
                        sums(L, winx, u, u % ES, SX, rows, L.winx_ready)
                with pe.Else():
                    pass

            grp = pe.alloc_register("pe_group")
            words = [pe.alloc_register(f"pe_meta{u}") for u in range(U + 1)]
            last = [pe.alloc_register(f"pe_last{n}") for n in range(2)]

            def node_group0():
                g = pe.snap(grp, min_val=0, max_val=NG - 1)
                pe.wait_ge(seeded, g * 2 + 2)
                for j in range(G):
                    pe.wait_ge(staged, g * G + (j + 1))
                    last = mm(degs[:, j, :], stage[:, j, 1, :], pick[:, :], start=True, stop=True)
                last.then_inc(deg_t, 1)
                for j in range(G):
                    mm(z(j), stage[:, j, 0, :], w0_sb[:, :], start=True, stop=False)
                    mm(z(j), stage[:, j, 1, :], wew[:, :], start=False, stop=True).then_inc(z_ready, 1)
                for j in range(G):
                    if j < G4:
                        pe.wait_ge(g_ready, g * G4 + (j + 1))
                    else:
                        pe.wait_ge(g_ready2, g + 1)
                    nc.tensor.transpose(gt[j // G4][:, (j % G4) * P:(j % G4 + 1) * P],
                                        gbuf[:, j, :], ident[:, :]).then_inc(g_t, 1)

            def node_group1():
                g = pe.snap(grp, min_val=0, max_val=NG - 1)
                for j in range(G):
                    pe.wait_ge(staged1, g * G + (j + 1))
                    mm(z(j), stage[:, j, 0, :], w1_sb[:, :], start=True, stop=True).then_inc(z1_ready, 1)

            def edge_loop(L, node_group):
                pe.reg_mov(extras, 0)
                pe.reg_mov(grp, 0)

                def body(i):
                    for u in range(U):
                        if u == U - 1:
                            next_words(pe, words, last, i)
                        chunk(L, i * U + u, u, P, i + 1, pe.snap(words[u] if u < U - 1 else last[0],
                                                                 min_val=0, max_val=N * P))
                    node_groups(pe, i, last[1], grp, node_group)

                load_meta(pe, words, 0)
                loop(pe, IT, body)
                chunk(L, NC, 0, TP, IT + 1, pe.snap(words[0], min_val=0, max_val=N * P))
                node_groups(pe, IT, words[U], grp, node_group)

            pe.wait_ge(wew_ok, 1)
            pe.wait_ge(pick_ok, 2)
            edge_loop(L0, node_group0)
            edge_loop(L1, node_group1)


_INS = ["x", "src", "dst", "edge_attr_64", "edge_weight", "L0_gnn_weight", "L0_gnn_weight_edge", "L0_gnn_bias",
        "L1_gnn_W", "L1_gnn_b"]


def kernel(**inputs):
    import numpy as _np
    import concourse.bacc as _bacc
    from concourse import mybir as _mybir
    from concourse.bass_utils import run_bass_kernel_spmd as _run

    nc = _bacc.Bacc("TRN2", target_bir_lowering=False, num_devices=1)
    arrays, args = {}, []
    for name in _INS:
        a = _np.ascontiguousarray(inputs[name])
        arrays[f"in_{name}"] = a
        args.append(nc.dram_tensor(f"in_{name}", a.shape, _mybir.dt.from_np(a.dtype), kind="ExternalInput").ap())
    n, d = inputs["x"].shape
    args.append(nc.dram_tensor("out_x", (n, d), _mybir.dt.float32, kind="ExternalOutput").ap())
    padded = -(-n // 128) * 128
    for name in ("h_table", "g_table"):
        args.append(nc.dram_tensor(name, (padded, d), _mybir.dt.float32).ap())
    gnn_two_layers(nc, *args)
    r = _run(nc, [arrays], core_ids=[0])
    return r.results[0]["out_x"]
```
